# Optimizing a Trainium2 kernel written in Bass

```python
import numpy as np
import jax
import jax.numpy as jnp

def _softmax(x, axis=-1):
    return jax.nn.softmax(x, axis=axis)

def _gelu(x):
    return jax.nn.gelu(x, approximate=True)

def _silu(x):
    return jax.nn.silu(x)

def _sigmoid(x):
    return jax.nn.sigmoid(x)

def _layernorm(x, axis=-1, eps=1e-05):
    m = jnp.mean(x, axis=axis, keepdims=True)
    v = jnp.var(x, axis=axis, keepdims=True)
    return (x - m) / jnp.sqrt(v + eps)

def _scatter_add(tgt, idx, src, axis=0):
    return tgt.at[idx].add(src)

def _segment_sum(src, seg, n):
    return jax.ops.segment_sum(src, seg, n)
kernel_name = 'mk_dlrm_tower_d1_rec_r8_5a7e67'

def setup_inputs(seed: int=0):
    np.random.seed(seed)
    _w = jnp.asarray

    def _rec_inputs():
        import jax
        import jax.numpy as jnp
        _tk = jax.random.key(seed)
        dense_ctx = jax.random.normal(jax.random.fold_in(_tk, 190), (2048, 16), jnp.float32)
        ids = jnp.stack([jax.random.randint(jax.random.fold_in(_tk, 200 + f), (2048,), 0, v, jnp.int32) for f, v in enumerate([1000, 12500, 125000, 1000, 1000, 1000, 1000, 1000, 1250, 125000, 1250, 1250, 12500, 125000, 1250, 125000, 125000, 1000, 1000, 12500, 1250, 1250, 1000, 1250, 12500, 12500, 1000, 1250, 12500, 12500, 125000, 1000])], axis=1)
        tbl_0 = 0.05 * jax.random.normal(jax.random.fold_in(_tk, 500 + 0), (1000, 16), jnp.float32)
        tbl_1 = 0.05 * jax.random.normal(jax.random.fold_in(_tk, 500 + 1), (12500, 16), jnp.float32)
        tbl_2 = 0.05 * jax.random.normal(jax.random.fold_in(_tk, 500 + 2), (125000, 16), jnp.float32)
        tbl_3 = 0.05 * jax.random.normal(jax.random.fold_in(_tk, 500 + 3), (1000, 16), jnp.float32)
        tbl_4 = 0.05 * jax.random.normal(jax.random.fold_in(_tk, 500 + 4), (1000, 16), jnp.float32)
        tbl_5 = 0.05 * jax.random.normal(jax.random.fold_in(_tk, 500 + 5), (1000, 16), jnp.float32)
        tbl_6 = 0.05 * jax.random.normal(jax.random.fold_in(_tk, 500 + 6), (1000, 16), jnp.float32)
        tbl_7 = 0.05 * jax.random.normal(jax.random.fold_in(_tk, 500 + 7), (1000, 16), jnp.float32)
        tbl_8 = 0.05 * jax.random.normal(jax.random.fold_in(_tk, 500 + 8), (1250, 16), jnp.float32)
        tbl_9 = 0.05 * jax.random.normal(jax.random.fold_in(_tk, 500 + 9), (125000, 16), jnp.float32)
        tbl_10 = 0.05 * jax.random.normal(jax.random.fold_in(_tk, 500 + 10), (1250, 16), jnp.float32)
        tbl_11 = 0.05 * jax.random.normal(jax.random.fold_in(_tk, 500 + 11), (1250, 16), jnp.float32)
        tbl_12 = 0.05 * jax.random.normal(jax.random.fold_in(_tk, 500 + 12), (12500, 16), jnp.float32)
        tbl_13 = 0.05 * jax.random.normal(jax.random.fold_in(_tk, 500 + 13), (125000, 16), jnp.float32)
        tbl_14 = 0.05 * jax.random.normal(jax.random.fold_in(_tk, 500 + 14), (1250, 16), jnp.float32)
        tbl_15 = 0.05 * jax.random.normal(jax.random.fold_in(_tk, 500 + 15), (125000, 16), jnp.float32)
        tbl_16 = 0.05 * jax.random.normal(jax.random.fold_in(_tk, 500 + 16), (125000, 16), jnp.float32)
        tbl_17 = 0.05 * jax.random.normal(jax.random.fold_in(_tk, 500 + 17), (1000, 16), jnp.float32)
        tbl_18 = 0.05 * jax.random.normal(jax.random.fold_in(_tk, 500 + 18), (1000, 16), jnp.float32)
        tbl_19 = 0.05 * jax.random.normal(jax.random.fold_in(_tk, 500 + 19), (12500, 16), jnp.float32)
        tbl_20 = 0.05 * jax.random.normal(jax.random.fold_in(_tk, 500 + 20), (1250, 16), jnp.float32)
        tbl_21 = 0.05 * jax.random.normal(jax.random.fold_in(_tk, 500 + 21), (1250, 16), jnp.float32)
        tbl_22 = 0.05 * jax.random.normal(jax.random.fold_in(_tk, 500 + 22), (1000, 16), jnp.float32)
        tbl_23 = 0.05 * jax.random.normal(jax.random.fold_in(_tk, 500 + 23), (1250, 16), jnp.float32)
        tbl_24 = 0.05 * jax.random.normal(jax.random.fold_in(_tk, 500 + 24), (12500, 16), jnp.float32)
        tbl_25 = 0.05 * jax.random.normal(jax.random.fold_in(_tk, 500 + 25), (12500, 16), jnp.float32)
        tbl_26 = 0.05 * jax.random.normal(jax.random.fold_in(_tk, 500 + 26), (1000, 16), jnp.float32)
        tbl_27 = 0.05 * jax.random.normal(jax.random.fold_in(_tk, 500 + 27), (1250, 16), jnp.float32)
        tbl_28 = 0.05 * jax.random.normal(jax.random.fold_in(_tk, 500 + 28), (12500, 16), jnp.float32)
        tbl_29 = 0.05 * jax.random.normal(jax.random.fold_in(_tk, 500 + 29), (12500, 16), jnp.float32)
        tbl_30 = 0.05 * jax.random.normal(jax.random.fold_in(_tk, 500 + 30), (125000, 16), jnp.float32)
        tbl_31 = 0.05 * jax.random.normal(jax.random.fold_in(_tk, 500 + 31), (1000, 16), jnp.float32)
        _rk = jax.random.fold_in(_tk, 7)
        W_top1 = 0.0441942 * jax.random.normal(jax.random.fold_in(_tk, 801), (512, 512), jnp.float32)
        W_top2 = 0.0441942 * jax.random.normal(jax.random.fold_in(_tk, 802), (512, 256), jnp.float32)
        W_top3 = 0.0625 * jax.random.normal(jax.random.fold_in(_tk, 803), (256, 1), jnp.float32)
        b_top1 = jnp.zeros((512,), jnp.float32)
        b_top2 = jnp.zeros((256,), jnp.float32)
        return (dense_ctx, ids, tbl_0, tbl_1, tbl_2, tbl_3, tbl_4, tbl_5, tbl_6, tbl_7, tbl_8, tbl_9, tbl_10, tbl_11, tbl_12, tbl_13, tbl_14, tbl_15, tbl_16, tbl_17, tbl_18, tbl_19, tbl_20, tbl_21, tbl_22, tbl_23, tbl_24, tbl_25, tbl_26, tbl_27, tbl_28, tbl_29, tbl_30, tbl_31, W_top1, b_top1, W_top2, b_top2, W_top3)
    dense_ctx, ids, tbl_0, tbl_1, tbl_2, tbl_3, tbl_4, tbl_5, tbl_6, tbl_7, tbl_8, tbl_9, tbl_10, tbl_11, tbl_12, tbl_13, tbl_14, tbl_15, tbl_16, tbl_17, tbl_18, tbl_19, tbl_20, tbl_21, tbl_22, tbl_23, tbl_24, tbl_25, tbl_26, tbl_27, tbl_28, tbl_29, tbl_30, tbl_31, W_top1, b_top1, W_top2, b_top2, W_top3 = _rec_inputs()

    def _L0_rec_setup():
        import jax, jax.numpy as jnp
        import numpy as np

        def _pair_indices(num_fields: int):
            row, col = ([], [])
            for i in range(num_fields - 1):
                for j in range(i + 1, num_fields):
                    row.append(i)
                    col.append(j)
            return (np.asarray(row, dtype=np.int32), np.asarray(col, dtype=np.int32))
        key = jax.random.key(seed)
        B, F, D = (2048, 32, 16)
        x = jax.random.normal(key, (B, F, D), dtype=jnp.float32)
        return {'x': x}
    _L0_rec_all = _L0_rec_setup()
    _L0_rec_in = {k: v for k, v in _L0_rec_all.items() if k in ()}
    del _L0_rec_all
    return {'dense_ctx': dense_ctx, 'ids': ids, 'tbl_0': tbl_0, 'tbl_1': tbl_1, 'tbl_2': tbl_2, 'tbl_3': tbl_3, 'tbl_4': tbl_4, 'tbl_5': tbl_5, 'tbl_6': tbl_6, 'tbl_7': tbl_7, 'tbl_8': tbl_8, 'tbl_9': tbl_9, 'tbl_10': tbl_10, 'tbl_11': tbl_11, 'tbl_12': tbl_12, 'tbl_13': tbl_13, 'tbl_14': tbl_14, 'tbl_15': tbl_15, 'tbl_16': tbl_16, 'tbl_17': tbl_17, 'tbl_18': tbl_18, 'tbl_19': tbl_19, 'tbl_20': tbl_20, 'tbl_21': tbl_21, 'tbl_22': tbl_22, 'tbl_23': tbl_23, 'tbl_24': tbl_24, 'tbl_25': tbl_25, 'tbl_26': tbl_26, 'tbl_27': tbl_27, 'tbl_28': tbl_28, 'tbl_29': tbl_29, 'tbl_30': tbl_30, 'tbl_31': tbl_31, 'W_top1': W_top1, 'b_top1': b_top1, 'W_top2': W_top2, 'b_top2': b_top2, 'W_top3': W_top3}

def reference(dense_ctx, ids, tbl_0, tbl_1, tbl_2, tbl_3, tbl_4, tbl_5, tbl_6, tbl_7, tbl_8, tbl_9, tbl_10, tbl_11, tbl_12, tbl_13, tbl_14, tbl_15, tbl_16, tbl_17, tbl_18, tbl_19, tbl_20, tbl_21, tbl_22, tbl_23, tbl_24, tbl_25, tbl_26, tbl_27, tbl_28, tbl_29, tbl_30, tbl_31, W_top1, b_top1, W_top2, b_top2, W_top3):
    import jax
    import jax.numpy as jnp

    def _L0_rec_ref(x):
        import jax, jax.numpy as jnp
        import numpy as np

        def _pair_indices(num_fields: int):
            row, col = ([], [])
            for i in range(num_fields - 1):
                for j in range(i + 1, num_fields):
                    row.append(i)
                    col.append(j)
            return (np.asarray(row, dtype=np.int32), np.asarray(col, dtype=np.int32))
        num_fields = x.shape[1]
        row, col = _pair_indices(num_fields)
        return jnp.sum(x[:, row, :] * x[:, col, :], axis=2)
    e = jnp.stack([tbl_0[ids[:, 0]], tbl_1[ids[:, 1]], tbl_2[ids[:, 2]], tbl_3[ids[:, 3]], tbl_4[ids[:, 4]], tbl_5[ids[:, 5]], tbl_6[ids[:, 6]], tbl_7[ids[:, 7]], tbl_8[ids[:, 8]], tbl_9[ids[:, 9]], tbl_10[ids[:, 10]], tbl_11[ids[:, 11]], tbl_12[ids[:, 12]], tbl_13[ids[:, 13]], tbl_14[ids[:, 14]], tbl_15[ids[:, 15]], tbl_16[ids[:, 16]], tbl_17[ids[:, 17]], tbl_18[ids[:, 18]], tbl_19[ids[:, 19]], tbl_20[ids[:, 20]], tbl_21[ids[:, 21]], tbl_22[ids[:, 22]], tbl_23[ids[:, 23]], tbl_24[ids[:, 24]], tbl_25[ids[:, 25]], tbl_26[ids[:, 26]], tbl_27[ids[:, 27]], tbl_28[ids[:, 28]], tbl_29[ids[:, 29]], tbl_30[ids[:, 30]], tbl_31[ids[:, 31]]], axis=1)
    z = _L0_rec_ref(e)
    z = z.reshape(z.shape[0], -1)
    h = jnp.concatenate([z, dense_ctx], axis=1)
    h = jnp.maximum(h @ W_top1 + b_top1, 0.0)
    h = jnp.maximum(h @ W_top2 + b_top2, 0.0)
    y = h @ W_top3
    return y

_drawn_inputs = setup_inputs


def setup_inputs(seed=0):
    import zlib

    import numpy as np

    out = dict(_drawn_inputs(seed))
    spreads = {'b_top1': (0.0, 0.1), 'b_top2': (0.0, 0.1)}
    factors = {'tbl_0': 4.938,
     'tbl_1': 4.823,
     'tbl_2': 4.627,
     'tbl_3': 4.486,
     'tbl_4': 3.969,
     'tbl_5': 5.084,
     'tbl_6': 4.379,
     'tbl_7': 4.032,
     'tbl_8': 4.652,
     'tbl_9': 4.4,
     'tbl_10': 4.424,
     'tbl_11': 4.3,
     'tbl_12': 4.211,
     'tbl_13': 4.053,
     'tbl_14': 4.747,
     'tbl_15': 4.431,
     'tbl_16': 4.121,
     'tbl_17': 4.773,
     'tbl_18': 4.191,
     'tbl_19': 4.4,
     'tbl_20': 4.221,
     'tbl_21': 4.446,
     'tbl_22': 4.568,
     'tbl_23': 4.702,
     'tbl_24': 4.664,
     'tbl_25': 4.218,
     'tbl_26': 4.504,
     'tbl_27': 4.493,
     'tbl_28': 4.703,
     'tbl_29': 4.443,
     'tbl_30': 4.5,
     'tbl_31': 4.818}
    for name, (base, spread) in spreads.items():
        noise = np.random.default_rng([zlib.crc32(name.encode()), seed]).standard_normal(out[name].shape)
        drawn = base * np.exp(spread * noise) if base else spread * noise
        out[name] = jnp.asarray(drawn.astype(out[name].dtype))
    for name, factor in factors.items():
        out[name] = (out[name] * factor).astype(out[name].dtype)
    return out
```

```python
def shifted_pairs(fields):
    pairs = []
    for k in range(1, fields // 2 + 1):
        for i in range(fields if 2 * k < fields else fields // 2):
            j = (i + k) % fields
            pairs.append((min(i, j), max(i, j)))
    return pairs


def build(nc, dense, ids, tables, w1, b1, w2, b2, w3, identity, out):
    import concourse.bass as bass
    from concourse import mybir
    from contextlib import ExitStack

    fp32, i32 = mybir.dt.float32, mybir.dt.int32
    ALU, ACT, AX = mybir.AluOpType, mybir.ActivationFunctionType, mybir.AxisListType

    P = 128
    B, F = ids.shape
    D = tables[0].shape[1]
    DENSE = dense.shape[1]
    H1, H2 = w2.shape
    NPAIR = F * (F - 1) // 2
    K1 = NPAIR + DENSE
    TILES = B // P
    GT = 4
    GROUPS = TILES // GT
    GB = GT * P
    KT1, KT2, KT3 = K1 // P, H1 // P, H2 // P
    SHIFTS = F // 2
    HALF = SHIFTS // 2
    WRAP = SHIFTS
    ROW = F * D

    ids_t = ids.rearrange("(u s p) f -> u s p f", p=P, s=2)
    dense_t = dense.rearrange("(u s p) f -> u s p f", p=P, s=2)

    ctx = ExitStack()
    with ctx:
        def sb(name, shape, dt=fp32):
            return ctx.enter_context(nc.sbuf_tensor(name, shape, dt))

        def pb(name, shape):
            return ctx.enter_context(nc.psum_tensor(name, shape, fp32))

        def sem(name):
            return ctx.enter_context(nc.semaphore(name))

        w1_sb = sb("w1_sb", [P, KT1, H1])
        w2_sb = sb("w2_sb", [P, KT2, H2])
        w3_sb = sb("w3_sb", [P, KT3])
        b1_sb = sb("b1_sb", [P, KT2])
        b2_sb = sb("b2_sb", [P, KT3])
        ident = sb("ident", [P, P])
        idx = [sb(f"idx{s}", [P, F], i32) for s in range(2)]
        emb = [sb(f"emb{s}", [P, (F + WRAP) * D]) for s in range(2)]
        prod = [sb(f"prod{s}", [P, HALF * ROW]) for s in range(2)]
        feat = [sb(f"feat{s}", [P, K1]) for s in range(2)]
        featT = sb("featT", [P, KT1, GB])
        h1 = sb("h1", [P, KT2, GB])
        h2 = sb("h2", [P, KT3, GB])
        y = sb("y", [1, B])

        ps_t = pb("ps_t", [P, KT1, P])
        ps_1 = [pb(f"ps_1{n}", [P, GB]) for n in range(KT2)]
        ps_2 = [pb(f"ps_2{n}", [P, GB]) for n in range(KT3)]
        ps_y = pb("ps_y", [P, GB])

        weights_in = sem("weights_in")
        idx_in = [sem(f"idx_in{s}") for s in range(2)]
        dense_in = [sem(f"dense_in{s}") for s in range(2)]
        gathered = [sem(f"gathered{s}") for s in range(2)]
        tiles_started = sem("tiles_started")
        wrapped = sem("wrapped")
        emb_slots = sem("emb_slots")
        feat_slots = sem("feat_slots")
        mult_a = sem("mult_a")
        mult_b = sem("mult_b")
        pairs_a = sem("pairs_a")
        pairs_b = sem("pairs_b")
        transposed = sem("transposed")
        featT_ready = sem("featT_ready")
        layer1 = sem("layer1")
        h1_ready = sem("h1_ready")
        layer2 = sem("layer2")
        h2_ready = sem("h2_ready")
        layer3 = sem("layer3")
        y_ready = sem("y_ready")
        stored = sem("stored")

        block = ctx.enter_context(nc.Block())

        @block.sync
        def _(sp):
            sp.sem_inc(feat_slots, 2)
            for tile_pair in range(1):
                for s in range(2):
                    sp.dma_start(idx[s][:, :], ids_t[0, s, :, :]).then_inc(idx_in[s], 16)
                    sp.dma_start(feat[s][:, NPAIR:K1], dense_t[0, s, :, :]).then_inc(dense_in[s], 16)
            sp.dma_start(ident[:, :], identity).then_inc(weights_in, 16)
            sp.dma_start(w1_sb[:, :, :], w1.rearrange("(k p) n -> p k n", p=P)).then_inc(weights_in, 16)
            sp.dma_start(w2_sb[:, :, :], w2.rearrange("(k p) n -> p k n", p=P)).then_inc(weights_in, 16)
            sp.dma_start(w3_sb[:, :], w3).then_inc(weights_in, 16)
            sp.dma_start(b1_sb[:, :], b1).then_inc(weights_in, 16)
            sp.dma_start(b2_sb[:, :], b2).then_inc(weights_in, 16)
            with sp.Fori(1, TILES // 2) as u:
                for s in range(2):
                    sp.wait_ge(gathered[s], u * (16 * F))
                    sp.dma_start(idx[s][:, :], ids_t[u, s, :, :]).then_inc(idx_in[s], 16)
                    sp.wait_ge(feat_slots, u * 2 + (s + 1))
                    sp.dma_start(feat[s][:, NPAIR:K1], dense_t[u, s, :, :]).then_inc(dense_in[s], 16)
            sp.wait_ge(y_ready, GROUPS)
            sp.dma_start(out.rearrange("b o -> o b"), y[0:1, :]).then_inc(stored, 16)
            sp.wait_ge(stored, 16)

        @block.gpsimd
        def _(pool):
            pool.sem_inc(emb_slots, 2)
            with pool.Fori(0, TILES, 2) as t:
                for s in range(2):
                    pool.wait_ge(idx_in[s], t * 8 + 16)
                    pool.wait_ge(emb_slots, t + (s + 1))
                    pool.sem_inc(tiles_started, 1)
                    for f in range(F):
                        nc.gpsimd.indirect_dma_start(
                            out=emb[s][:, f * D:(f + 1) * D], out_offset=None, in_=tables[f],
                            in_offset=bass.IndirectOffsetOnAxis(ap=idx[s][:, f:f + 1], axis=0),
                        ).then_inc(gathered[s], 16)

        def window(t, s, first, step, count, size):
            a = t[s][:, :]
            return bass.AP(a.tensor, a.offset + first, [list(a.ap[0]), [step, count], [1, size]])

        @block.vector
        def _(dve):
            with dve.Fori(0, TILES, 2) as t:
                for s in range(2):
                    e = emb[s]
                    dve.wait_ge(wrapped, t + (s + 1))
                    dve.wait_ge(gathered[s], t * (8 * F) + 16 * F)
                    nc.vector.tensor_tensor(
                        prod[0][:, :].rearrange("p (k r) -> p k r", k=HALF),
                        window(emb, s, 0, 0, HALF, ROW), window(emb, s, D, D, HALF, ROW), ALU.mult).then_inc(mult_a, 1)
                    nc.vector.tensor_tensor(
                        prod[1][:, 0:(HALF - 1) * ROW].rearrange("p (k r) -> p k r", k=HALF - 1),
                        window(emb, s, 0, 0, HALF - 1, ROW),
                        window(emb, s, (HALF + 1) * D, D, HALF - 1, ROW), ALU.mult).then_inc(mult_b, 1)
                    last = nc.vector.tensor_tensor(
                        prod[1][:, (HALF - 1) * ROW:(HALF - 1) * ROW + ROW // 2],
                        e[:, 0:ROW // 2], e[:, ROW // 2:ROW], ALU.mult)
                    last.then_inc(mult_b, 1)
                    dve.wait_ge(feat_slots, t + (s + 1))
                    dve.wait_ge(mult_a, t + (s + 1))
                    nc.vector.tensor_reduce(
                        feat[s][:, 0:HALF * F], prod[0][:, :].rearrange("p (q d) -> p q d", d=D),
                        AX.X, ALU.add).then_inc(pairs_a, 1)
                    dve.wait_ge(mult_b, t * 2 + (2 * s + 2))
                    nc.vector.tensor_reduce(
                        feat[s][:, HALF * F:NPAIR],
                        prod[1][:, 0:(NPAIR - HALF * F) * D].rearrange("p (q d) -> p q d", d=D),
                        AX.X, ALU.add).then_inc(pairs_b, 1)
                    dve.wait_ge(pairs_a, t + (s + 1))
                    dve.wait_ge(pairs_b, t + (s + 1))
                    dve.sem_inc(emb_slots, 1)

        @block.tensor
        def _(pe):
            pe.wait_ge(weights_in, 6 * 16)
            with pe.Fori(0, GROUPS) as g:
                for q in range(GT):
                    s = q % 2
                    pe.wait_ge(pairs_a, g * GT + (q + 1))
                    pe.wait_ge(pairs_b, g * GT + (q + 1))
                    pe.wait_ge(dense_in[s], g * (GT * 8) + 16 * (q // 2 + 1))
                    if q:
                        pe.wait_ge(featT_ready, g * GT + q)
                    for k in range(KT1):
                        last = nc.tensor.transpose(ps_t[:, k, :], feat[s][:, k * P:(k + 1) * P], ident[:, :])
                    last.then_inc(transposed, 1)
                pe.wait_ge(featT_ready, g * GT + GT)
                for n in range(KT2):
                    for k in range(KT1):
                        last = nc.tensor.matmul(ps_1[n][:, :], w1_sb[:, k, n * P:(n + 1) * P], featT[:, k, :],
                                                start=(k == 0), stop=(k == KT1 - 1))
                    last.then_inc(layer1, 1)
                for n in range(KT3):
                    if n == 0:
                        pe.wait_ge(h1_ready, g * KT2 + KT2)
                    for k in range(KT2):
                        last = nc.tensor.matmul(ps_2[n][:, :], w2_sb[:, k, n * P:(n + 1) * P], h1[:, k, :],
                                                start=(k == 0), stop=(k == KT2 - 1))
                    last.then_inc(layer2, 1)
                pe.wait_ge(h2_ready, g * KT3 + KT3)
                for k in range(KT3):
                    last = nc.tensor.matmul(ps_y[0:1, :], w3_sb[:, k:k + 1], h2[:, k, :],
                                            start=(k == 0), stop=(k == KT3 - 1))
                last.then_inc(layer3, 1)
                pe.wait_ge(y_ready, g + 1)

        @block.scalar
        def _(act):
            with act.Fori(0, GROUPS) as g:
                for q in range(GT):
                    s = q % 2
                    act.wait_ge(gathered[s], g * (GT * 8 * F) + 16 * F * (q // 2 + 1))
                    nc.scalar.copy(emb[s][:, ROW:ROW + WRAP * D], emb[s][:, 0:WRAP * D]).then_inc(wrapped, 1)
                    act.wait_ge(transposed, g * GT + (q + 1))
                    act.sem_inc(feat_slots, 1)
                    nc.scalar.copy(featT[:, :, q * P:(q + 1) * P], ps_t[:, :, :]).then_inc(featT_ready, 1)
                for n in range(KT2):
                    act.wait_ge(layer1, g * KT2 + (n + 1))
                    nc.scalar.activation(h1[:, n, :], ps_1[n][:, :], ACT.Relu, bias=b1_sb[:, n:n + 1]).then_inc(h1_ready, 1)
                for n in range(KT3):
                    act.wait_ge(layer2, g * KT3 + (n + 1))
                    nc.scalar.activation(h2[:, n, :], ps_2[n][:, :], ACT.Relu, bias=b2_sb[:, n:n + 1]).then_inc(h2_ready, 1)
                act.wait_ge(layer3, g + 1)
                nc.scalar.copy(y[0:1, bass.ts(g, GB)], ps_y[0:1, :]).then_inc(y_ready, 1)


def kernel(**inputs):
    import numpy as np
    import concourse.bacc as bacc
    from concourse import mybir
    from concourse.bass_utils import run_bass_kernel_spmd as run

    F = inputs["ids"].shape[1]
    pairs = shifted_pairs(F)
    row_of = {}
    for i in range(F - 1):
        for j in range(i + 1, F):
            row_of[i, j] = len(row_of)
    w1 = np.asarray(inputs["W_top1"])
    order = [row_of[p] for p in pairs] + list(range(len(pairs), w1.shape[0]))
    b1, b2, w3 = (np.asarray(inputs[k]) for k in ("b_top1", "b_top2", "W_top3"))
    host = {
        "dense": np.asarray(inputs["dense_ctx"]),
        "ids": np.asarray(inputs["ids"]),
        "w1": np.ascontiguousarray(w1[order]),
        "b1": np.ascontiguousarray(b1.reshape(-1, 128).T),
        "w2": np.asarray(inputs["W_top2"]),
        "b2": np.ascontiguousarray(b2.reshape(-1, 128).T),
        "w3": np.ascontiguousarray(w3.reshape(-1, 128).T),
        "identity": np.eye(128, dtype=np.float32),
    }
    for f in range(F):
        host[f"tbl_{f}"] = np.asarray(inputs[f"tbl_{f}"])

    nc = bacc.Bacc("TRN2", target_bir_lowering=False, num_devices=1)
    ap = {k: nc.dram_tensor(f"in_{k}", v.shape, mybir.dt.from_np(v.dtype), kind="ExternalInput").ap()
          for k, v in host.items()}
    B = host["ids"].shape[0]
    out = nc.dram_tensor("out_y", (B, 1), mybir.dt.float32, kind="ExternalOutput").ap()
    build(nc, ap["dense"], ap["ids"], [ap[f"tbl_{f}"] for f in range(F)],
          ap["w1"], ap["b1"], ap["w2"], ap["b2"], ap["w3"], ap["identity"], out)
    r = run(nc, [{f"in_{k}": v for k, v in host.items()}], core_ids=[0])
    return r.results[0]["out_y"]
```

```python
P = 128
SPAN = 256
MOST_ROWS = 1280


def field_order(sizes):
    small = sorted((f for f, v in enumerate(sizes) if v <= MOST_ROWS), key=lambda f: (-(-sizes[f] // SPAN), f))
    return small, [f for f in range(len(sizes)) if f not in small]


def shifted_pairs(fields):
    return [(i, (i + k) % fields) for k in range(1, fields // 2 + 1)
            for i in range(fields if 2 * k < fields else fields // 2)]


def build(nc, dense_T, ids_flat, ids_small, ids_large, large, tbl, widths, w1, b1, w2, b2, w3, consts, out):
    import concourse.bass as bass
    from concourse import mybir
    from contextlib import ExitStack

    fp32, bf16, i32 = mybir.dt.float32, mybir.dt.bfloat16, mybir.dt.int32
    ALU, ACT = mybir.AluOpType, mybir.ActivationFunctionType

    B, L = ids_large.shape
    S = len(widths)
    F = S + L
    D = large[0].shape[1]
    DENSE = dense_T.shape[0]
    H1, H2 = w2.shape
    TILES = B // P
    GT = 4
    GROUPS = TILES // GT
    GB = GT * P
    HB = 2 * P
    HALVES = B // HB
    NPAIR = F * (F - 1) // 2
    KT1, KT2, KT3 = (NPAIR + DENSE) // P, H1 // P, H2 // P
    WRAP = F // 2
    ROW = F * D
    SHIFTS = P // F
    CAND = sum(widths)
    HIGHS = max(widths) // D
    FEW = min(widths) // D
    N_FEW = sum(w == FEW * D for w in widths)
    COLS_FEW = N_FEW * FEW * D
    OFF = [sum(widths[:f]) for f in range(S)]

    ctx = ExitStack()
    with ctx:
        def sb(name, shape, dt=fp32):
            return ctx.enter_context(nc.sbuf_tensor(name, shape, dt))

        def pb(name, shape):
            return ctx.enter_context(nc.psum_tensor(name, shape, fp32))

        def sem(name):
            return ctx.enter_context(nc.semaphore(name))

        w1_sb = sb("w1_sb", [P, KT1, H1])
        w2_sb = sb("w2_sb", [P, KT2, H2])
        w3_sb = sb("w3_sb", [P, KT3])
        b1_sb = sb("b1_sb", [P, KT2])
        b2_sb = sb("b2_sb", [P, KT3])
        consts_sb = sb("consts_sb", [P, consts.shape[1]])
        ident = consts_sb[:, 0:P]
        low_no = consts_sb[:, P:P + 2]
        high_no = consts_sb[:, P + 2:P + 2 + HIGHS]
        idx = [sb(f"idx{s}", [P, L], i32) for s in range(GT)]
        emb = [sb(f"emb{s}", [P, (F + WRAP) * D]) for s in range(GT)]
        prod = sb("prod", [P, KT1, P * D])
        featT = sb("featT", [P, KT1, B])
        h1 = sb("h1", [P, KT2, GB])
        h2 = sb("h2", [P, KT3, GB])
        y = sb("y", [1, B])
        ids_f = sb("ids_f", [P, S * B // P], i32)
        low_b = sb("low_b", [P, S * B // P], bf16)
        ids_s = sb("ids_s", [P, TILES, S], i32)
        high = sb("high", [P, TILES, S], i32)
        mask = sb("mask", [P, TILES * S, HIGHS])
        masked = sb("masked", [P, CAND])
        low_all = [sb(f"low_all{s}", [P, S * HB], bf16) for s in range(2)]
        onehot = [sb(f"onehot{s}", [P, 2, S * HB], bf16) for s in range(2)]
        parts = sb("parts", [P, 3, 2 * CAND], bf16)
        prod_flat = prod[:, :, :].rearrange("p k c -> p (k c)")
        tbl_sb = prod_flat[:, 0:2 * CAND]
        rest = prod_flat[:, 2 * CAND:4 * CAND]
        low_dram = nc.dram_tensor("low_dram", (S * B,), bf16).ap()

        cand = pb("cand", [P, 3 * 512])
        pairsT = [pb(f"pairsT{s}", [P, KT1, P]) for s in range(2)]
        dense_ps = [pb(f"dense_ps{s}", [P, GB]) for s in range(2)]
        y_ps = pb("y_ps", [P, GB])

        prep_in = sem("prep_in")
        tbl_in = sem("tbl_in")
        weights_in = sem("weights_in")
        idx_in = [sem(f"idx_in{s}") for s in range(GT)]
        gathered = [sem(f"gathered{s}") for s in range(GT)]
        low_int = sem("low_int")
        low_ready = sem("low_ready")
        low_stored = sem("low_stored")
        low_in = [sem(f"low_in{s}") for s in range(2)]
        high_ready = sem("high_ready")
        part_ready = sem("part_ready")
        rest_ready = sem("rest_ready")
        onehot_ready = sem("onehot_ready")
        cand_ready = sem("cand_ready")
        mask_ready = sem("mask_ready")
        cand_used = sem("cand_used")
        kept = sem("kept")
        wrapped = sem("wrapped")
        multiplied = sem("multiplied")
        prod_used = sem("prod_used")
        tiles_started = sem("tiles_started")
        featT_ready = sem("featT_ready")
        summed = sem("summed")
        dense_done = sem("dense_done")
        dense_out = sem("dense_out")
        y_done = sem("y_done")
        y_out = sem("y_out")
        stored = sem("stored")

        ND = KT2 + KT3

        block = ctx.enter_context(nc.Block())

        @block.sync
        def _(sp):
            idx_t = ids_large.rearrange("(t p) f -> t p f", p=P)
            sp.dma_start(ids_f[:, :], ids_flat).then_inc(prep_in, 16)
            for t in range(GT):
                sp.dma_start(idx[t][:, :], idx_t[t, :, :]).then_inc(idx_in[t], 16)
            sp.dma_start(tbl_sb, tbl).then_inc(tbl_in, 16)
            sp.wait_ge(low_ready, 1)
            sp.dma_start(low_dram.rearrange("(p c) -> p c", p=P), low_b[:, :]).then_inc(low_stored, 16)
            sp.dma_start(consts_sb[:, :], consts).then_inc(prep_in, 16)
            sp.dma_start(ids_s[:, :, :], ids_small.rearrange("(t p) f -> p t f", p=P)).then_inc(prep_in, 16)
            sp.wait_ge(low_stored, 16)

            def load_low(h):
                row = low_dram[h * S * HB:(h + 1) * S * HB]
                sp.dma_start(low_all[h % 2][:, :], row.partition_broadcast(P)).then_inc(low_in[h % 2], 16)

            load_low(0)
            load_low(1)
            sp.dma_start(featT[P - DENSE:P, KT1 - 1, :], dense_T).then_inc(weights_in, 16)
            sp.dma_start(w1_sb[:, :, :], w1.rearrange("(k p) n -> p k n", p=P)).then_inc(weights_in, 16)
            sp.dma_start(w2_sb[:, :, :], w2.rearrange("(k p) n -> p k n", p=P)).then_inc(weights_in, 16)
            sp.dma_start(w3_sb[:, :], w3).then_inc(weights_in, 16)
            sp.dma_start(b1_sb[:, :], b1).then_inc(weights_in, 16)
            sp.dma_start(b2_sb[:, :], b2).then_inc(weights_in, 16)
            for h in range(2, HALVES):
                sp.wait_ge(onehot_ready, 2 * (h - 1))
                load_low(h)
                for t in (2 * h, 2 * h + 1):
                    sp.wait_ge(gathered[t % GT], t // GT * 16 * L)
                    sp.dma_start(idx[t % GT][:, :], idx_t[t, :, :]).then_inc(idx_in[t % GT], 16)
            sp.wait_ge(y_out, 1 + GROUPS)
            sp.dma_start(out.rearrange("b o -> o b"), y[0:1, :]).then_inc(stored, 16)
            sp.wait_ge(stored, 16)

        @block.gpsimd
        def _(pool):
            with pool.Fori(0, GROUPS) as g:
                for q in range(GT):
                    pool.wait_ge(multiplied, g * (GT * KT1) + KT1 * (q + 1))
                    pool.wait_ge(idx_in[q], g * 16 + 16)
                    pool.sem_inc(tiles_started, 1)
                    for f in range(L):
                        nc.gpsimd.indirect_dma_start(
                            out=emb[q][:, (S + f) * D:(S + f + 1) * D], out_offset=None, in_=large[f],
                            in_offset=bass.IndirectOffsetOnAxis(ap=idx[q][:, f:f + 1], axis=0),
                        ).then_inc(gathered[q], 16)

        def window(t, first, step, count, size):
            a = t[:, :]
            return bass.AP(a.tensor, a.offset + first, [list(a.ap[0]), [step, count], [1, size]])

        @block.vector
        def _(dve):
            dve.sem_inc(multiplied, GT * KT1)
            dve.sem_inc(cand_used, 1)
            dve.wait_ge(prep_in, 16)
            nc.vector.tensor_single_scalar(ids_f[:, :], ids_f[:, :], SPAN - 1, ALU.bitwise_and).then_inc(low_int, 1)
            dve.wait_ge(low_int, 1)
            nc.vector.tensor_copy(low_b[:, :], ids_f[:, :]).then_inc(low_ready, 1)
            dve.wait_ge(prep_in, 3 * 16)
            nc.vector.tensor_single_scalar(high[:, :, :], ids_s[:, :, :], SPAN.bit_length() - 1,
                                           ALU.logical_shift_right).then_inc(high_ready, 1)
            dve.wait_ge(high_ready, 1)
            nc.vector.tensor_tensor(
                mask[:, :, :], high[:, :, :].rearrange("p t f -> p (t f)").unsqueeze(2).to_broadcast([P, TILES * S, HIGHS]),
                high_no.unsqueeze(1).to_broadcast([P, TILES * S, HIGHS]), ALU.is_equal).then_inc(mask_ready, 1)
            dve.wait_ge(part_ready, 1)
            nc.vector.tensor_tensor(rest, tbl_sb, parts[:, 0, :], ALU.subtract).then_inc(rest_ready, 1)

            def make_onehot(half, s):
                dve.wait_ge(low_in[s], half * 8 + (16 - 8 * s))
                for k in range(2):
                    nc.vector.tensor_single_scalar(onehot[s][:, k, :], low_all[s][:, :], low_no[:, k:k + 1],
                                                   ALU.is_equal).then_inc(onehot_ready, 1)

            def keep(t, q):
                e = emb[q]
                kinds = [(0, N_FEW, 0, FEW), (N_FEW, S - N_FEW, COLS_FEW, HIGHS)]
                tile_mask = mask[:, :, :].rearrange("p (t f) h -> p t f h", f=S)[:, t, :, :]
                dve.wait_ge(cand_ready, t + 1)
                for f0, n, c0, m in kinds:
                    last = nc.vector.tensor_tensor(
                        masked[:, c0:c0 + n * m * D].rearrange("p (f h d) -> p f h d", h=m, d=D),
                        cand[:, c0:c0 + n * m * D].rearrange("p (f h d) -> p f h d", h=m, d=D),
                        tile_mask[:, f0:f0 + n, 0:m].unsqueeze(3).to_broadcast([P, n, m, D]), ALU.mult)
                last.then_inc(cand_used, 1)
                dve.wait_ge(cand_used, t + 2)
                for f0, n, c0, m in kinds:
                    last = nc.vector.tensor_reduce(
                        e[:, f0 * D:(f0 + n) * D].rearrange("p (f d) -> p f d", d=D),
                        masked[:, c0:c0 + n * m * D].rearrange("p (f h d) -> p f d h", h=m, d=D),
                        mybir.AxisListType.X, ALU.add)
                last.then_inc(kept, 1)
                dve.wait_ge(kept, t + 1)
                nc.vector.tensor_copy(e[:, ROW:ROW + WRAP * D], e[:, 0:WRAP * D]).then_inc(wrapped, 1)

            def multiply(t, g, q):
                e = emb[q]
                dve.wait_ge(wrapped, t + 1)
                dve.wait_ge(gathered[q], g * (16 * L) + 16 * L)
                for k in range(KT1):
                    dve.wait_ge(prod_used, t * KT1 + (k + 1))
                    first = (k * SHIFTS + 1) * D
                    whole = SHIFTS if k < KT1 - 1 else SHIFTS - 1
                    last = nc.vector.tensor_tensor(
                        prod[:, k, 0:whole * ROW].rearrange("p (k r) -> p k r", r=ROW),
                        window(e, 0, 0, whole, ROW), window(e, first, D, whole, ROW), ALU.mult)
                    if whole < SHIFTS:
                        last = nc.vector.tensor_tensor(prod[:, k, whole * ROW:whole * ROW + ROW // 2],
                                                       e[:, 0:ROW // 2], e[:, ROW // 2:ROW], ALU.mult)
                    last.then_inc(multiplied, 1)

            make_onehot(0, 0)
            dve.wait_ge(part_ready, 2)
            dve.wait_ge(rest_ready, 1)
            nc.vector.tensor_tensor(parts[:, 2, :], rest, parts[:, 1, :], ALU.subtract).then_inc(part_ready, 1)
            dve.wait_ge(part_ready, 3)
            dve.wait_ge(mask_ready, 1)
            keep(0, 0)

            def group(g, last):
                for q in range(GT):
                    t = g * GT + q
                    if q % 2 == 0 and not (last and q == 2):
                        if not (isinstance(g, int) and g == 0 and q == 0):
                            dve.wait_ge(cand_ready, t)
                        make_onehot(g * 2 + (q // 2 + 1), (q // 2 + 1) % 2)
                    multiply(t, g, q)
                    if not (last and q == GT - 1):
                        keep(t + 1, (q + 1) % GT)

            group(0, False)
            with dve.Fori(1, GROUPS - 1) as g:
                group(g, False)
            group(GROUPS - 1, True)

        @block.tensor
        def _(pe):
            pe.sem_inc(prod_used, KT1)

            def look_up(t, q):
                pe.wait_ge(onehot_ready, t + 2 - q % 2)
                pe.wait_ge(cand_used, t + 1)
                s, c = q // 2, (q % 2) * P
                for f in range(S):
                    for k in range(2):
                        for part in range(3):
                            last = nc.tensor.matmul(
                                cand[:, OFF[f]:OFF[f] + widths[f]],
                                onehot[s][:, k, f * HB + c:f * HB + c + P],
                                parts[:, part, k * CAND + OFF[f]:k * CAND + OFF[f] + widths[f]],
                                start=(k == 0 and part == 0), stop=(k == 1 and part == 2))
                last.then_inc(cand_ready, 1)

            def transpose_and_sum(t, q):
                pe.wait_ge(featT_ready, t + 1)
                for k in range(KT1):
                    pe.wait_ge(multiplied, t * KT1 + (GT * KT1 + k + 1))
                    n = min(P, NPAIR - k * P)
                    src = prod[:, k, 0:n * D].rearrange("p (q d) -> p d q", d=D)
                    for d in range(D):
                        last = nc.tensor.matmul(pairsT[q % 2][0:n, k, :], src[:, d, :], ident, is_transpose=True,
                                                start=(d == 0), stop=(d == D - 1))
                    last.then_inc(prod_used, 1)

            def layer_12(G, n):
                pe.wait_ge(dense_out, G * ND + (n + 1))
                if n < KT2:
                    w, x, kt, m = w1_sb, featT[:, :, bass.ts(G, GB)], KT1, n
                    if n == 0:
                        pe.wait_ge(featT_ready, G * GT + (GT + 2))
                else:
                    w, x, kt, m = w2_sb, h1[:, :, :], KT2, n - KT2
                    pe.wait_ge(dense_out, G * ND + (KT2 + 2))
                for k in range(kt):
                    last = nc.tensor.matmul(dense_ps[n % 2][:, :], w[:, k, m * P:(m + 1) * P], x[:, k, :],
                                            start=(k == 0), stop=(k == kt - 1))
                last.then_inc(dense_done, 1)

            def layer_3(G):
                pe.wait_ge(dense_out, G * ND + (ND + 2))
                pe.wait_ge(y_out, G + 1)
                for k in range(KT3):
                    last = nc.tensor.matmul(y_ps[0:1, :], w3_sb[:, k:k + 1], h2[:, k, :],
                                            start=(k == 0), stop=(k == KT3 - 1))
                last.then_inc(y_done, 1)

            def dense_piece(G, q):
                if q < GT - 1:
                    layer_12(G, 2 * q)
                    layer_12(G, 2 * q + 1)
                else:
                    layer_3(G)

            pe.wait_ge(part_ready, 3)
            look_up(0, 0)
            pe.wait_ge(weights_in, 6 * 16)
            pe.wait_ge(prep_in, 3 * 16)

            def group(g, first, last):
                for q in range(GT):
                    t = g * GT + q
                    if not (last and q == GT - 1):
                        look_up(t + 1, (q + 1) % GT)
                    transpose_and_sum(t, q)
                    if not first:
                        dense_piece(g - 1, q)

            group(0, True, False)
            with pe.Fori(1, GROUPS - 1) as g:
                group(g, False, False)
            group(GROUPS - 1, False, True)
            for q in range(GT):
                dense_piece(GROUPS - 1, q)

        @block.scalar
        def _(act):
            act.sem_inc(featT_ready, 2)
            act.sem_inc(dense_out, 2)
            act.sem_inc(y_out, 1)
            act.wait_ge(tbl_in, 16)
            nc.scalar.copy(parts[:, 0, :], tbl_sb).then_inc(part_ready, 1)
            act.wait_ge(rest_ready, 1)
            nc.scalar.copy(parts[:, 1, :], rest).then_inc(part_ready, 1)

            def store_pairs(t, q):
                act.wait_ge(prod_used, t * KT1 + 2 * KT1)
                rows = NPAIR - (KT1 - 1) * P
                x = featT[:, :, :].rearrange("p k (t c) -> p k t c", c=P)
                nc.scalar.copy(x[:, 0:KT1 - 1, t, :], pairsT[q % 2][:, 0:KT1 - 1, :])
                nc.scalar.copy(x[0:rows, KT1 - 1, t, :], pairsT[q % 2][0:rows, KT1 - 1, :]).then_inc(featT_ready, 1)

            def dense_piece(G, q):
                if q < GT - 1:
                    for n in (2 * q, 2 * q + 1):
                        act.wait_ge(dense_done, G * ND + (n + 1))
                        o, b = (h1[:, n, :], b1_sb[:, n:n + 1]) if n < KT2 else (h2[:, n - KT2, :], b2_sb[:, n - KT2:n - KT2 + 1])
                        nc.scalar.activation(o, dense_ps[n % 2][:, :], ACT.Relu, bias=b).then_inc(dense_out, 1)
                else:
                    act.wait_ge(y_done, G + 1)
                    nc.scalar.copy(y[0:1, bass.ts(G, GB)], y_ps[0:1, :]).then_inc(y_out, 1)

            def group(g, first):
                for q in range(GT):
                    t = g * GT + q
                    store_pairs(t, q)
                    if not first:
                        dense_piece(g - 1, q)

            group(0, True)
            with act.Fori(1, GROUPS) as g:
                group(g, False)
            for q in range(GT):
                dense_piece(GROUPS - 1, q)


def kernel(**inputs):
    import numpy as np
    import concourse.bacc as bacc
    from concourse import mybir
    from concourse.bass_utils import run_bass_kernel_spmd as run

    ids = np.asarray(inputs["ids"])
    B, F = ids.shape
    tables = [np.asarray(inputs[f"tbl_{f}"]) for f in range(F)]
    D = tables[0].shape[1]
    small, large = field_order([t.shape[0] for t in tables])
    order = small + large
    row_of = {}
    for i in range(F - 1):
        for j in range(i + 1, F):
            row_of[i, j] = len(row_of)
    w1 = np.asarray(inputs["W_top1"])
    rows = [row_of[min(order[i], order[j]), max(order[i], order[j])] for i, j in shifted_pairs(F)]
    rows += range(len(rows), w1.shape[0])

    highs = [-(-tables[f].shape[0] // SPAN) for f in small]
    blocks = []
    for f, n in zip(small, highs):
        padded = np.zeros((n * SPAN, D), np.float32)
        padded[:tables[f].shape[0]] = tables[f]
        blocks.append(padded.reshape(n, 2, P, D).transpose(2, 1, 0, 3).reshape(P, 2, n * D))
    tbl = np.concatenate(blocks, axis=2)

    HB = 2 * P
    ids_flat = np.ascontiguousarray(ids[:, small].reshape(B // HB, HB, len(small)).transpose(0, 2, 1)).reshape(P, -1)
    consts = np.zeros((P, P + 2 + max(highs)), np.float32)
    consts[:, :P] = np.eye(P, dtype=np.float32)
    consts[:, P] = np.arange(P)
    consts[:, P + 1] = np.arange(P, 2 * P)
    consts[:, P + 2:] = np.arange(max(highs))
    b1, b2, w3 = (np.asarray(inputs[k]) for k in ("b_top1", "b_top2", "W_top3"))
    host = {
        "dense_T": np.ascontiguousarray(np.asarray(inputs["dense_ctx"]).T),
        "ids_flat": ids_flat,
        "ids_small": np.ascontiguousarray(ids[:, small]),
        "ids_large": np.ascontiguousarray(ids[:, large]),
        "tbl": tbl.reshape(P, -1),
        "w1": np.ascontiguousarray(w1[rows]),
        "b1": np.ascontiguousarray(b1.reshape(-1, P).T),
        "w2": np.asarray(inputs["W_top2"]),
        "b2": np.ascontiguousarray(b2.reshape(-1, P).T),
        "w3": np.ascontiguousarray(w3.reshape(-1, P).T),
        "consts": consts,
    }
    names = list(host)
    for f in large:
        host[f"tbl_{f}"] = tables[f]

    nc = bacc.Bacc("TRN2", target_bir_lowering=False, num_devices=1)
    ap = {k: nc.dram_tensor(f"in_{k}", v.shape, mybir.dt.from_np(v.dtype), kind="ExternalInput").ap()
          for k, v in host.items()}
    out = nc.dram_tensor("out_y", (B, 1), mybir.dt.float32, kind="ExternalOutput").ap()
    build(nc, ap["dense_T"], ap["ids_flat"], ap["ids_small"], ap["ids_large"], [ap[f"tbl_{f}"] for f in large],
          ap["tbl"], [n * D for n in highs], ap["w1"], ap["b1"], ap["w2"], ap["b2"], ap["w3"], ap["consts"], out)
    r = run(nc, [{f"in_{k}": v for k, v in host.items()}], core_ids=[0])
    return r.results[0]["out_y"]
```

```python
P = 128
SPAN = 256
MOST_ROWS = 1280
MOST_SMALL = 19


def field_order(sizes):
    small = sorted((f for f, v in enumerate(sizes) if v <= MOST_ROWS), key=lambda f: (-(-sizes[f] // SPAN), f))
    small = small[:MOST_SMALL]
    return small, [f for f in range(len(sizes)) if f not in small]


def shifted_pairs(fields):
    return [(i, (i + k) % fields) for k in range(1, fields // 2 + 1)
            for i in range(fields if 2 * k < fields else fields // 2)]


def build(nc, dense, ids_flat, ids_small, ids_large, large, tbl, widths, w1, b1, w2, b2, w3, consts, out):
    import concourse.bass as bass
    from concourse import mybir
    from contextlib import ExitStack

    fp32, fp32r, bf16, i32 = mybir.dt.float32, mybir.dt.float32r, mybir.dt.bfloat16, mybir.dt.int32
    ALU, ACT = mybir.AluOpType, mybir.ActivationFunctionType

    B, L = ids_large.shape
    S = len(widths)
    F = S + L
    D = large[0].shape[1]
    DENSE = dense.shape[1]
    H1, H2 = w2.shape
    TILES = B // P
    GT = 4
    GROUPS = TILES // GT
    GB = GT * P
    HB = 2 * P
    HALVES = B // HB
    AHEAD = GT - 1
    NPAIR = F * (F - 1) // 2
    KT1, KT2, KT3 = (NPAIR + DENSE) // P, H1 // P, H2 // P
    WRAP = F // 2
    ROW = F * D
    SHIFTS = P // F
    CAND = sum(widths)
    HIGHS = max(widths) // D
    FEW = min(widths) // D
    N_FEW = sum(w == FEW * D for w in widths)
    COLS_FEW = N_FEW * FEW * D
    OFF = [sum(widths[:f]) for f in range(S)]

    ctx = ExitStack()
    with ctx:
        def sb(name, shape, dt=fp32):
            return ctx.enter_context(nc.sbuf_tensor(name, shape, dt))

        def pb(name, shape):
            return ctx.enter_context(nc.psum_tensor(name, shape, fp32))

        def sem(name):
            return ctx.enter_context(nc.semaphore(name))

        w1_sb = sb("w1_sb", [P, 2, KT1 * H1], fp32r)
        w2_sb = sb("w2_sb", [P, 2, KT2 * H2], fp32r)
        feat = sb("feat", [P, 2, 2, KT1, GB], fp32r)
        h1 = sb("h1", [P, 2, KT2, GB], fp32r)
        h1_whole = [sb(f"h1_whole{s}", [P, GB]) for s in range(2)]
        w3_sb = sb("w3_sb", [P, KT3])
        b1_sb = sb("b1_sb", [P, KT2])
        b2_sb = sb("b2_sb", [P, KT3])
        consts_sb = sb("consts_sb", [P, consts.shape[1]])
        ident = consts_sb[:, 0:P]
        low_no = consts_sb[:, P:P + 2]
        minus_low_no = consts_sb[:, P + 2:P + 3]
        one = consts_sb[:, P + 3:P + 4]
        high_no = consts_sb[:, P + 4:P + 4 + HIGHS]
        idx = [sb(f"idx{s}", [P, L], i32) for s in range(GT)]
        emb = [sb(f"emb{s}", [P, (F + WRAP) * D]) for s in range(GT)]
        prod = sb("prod", [P, KT1, P * D])
        h2 = sb("h2", [P, KT3, GB])
        y = sb("y", [P, TILES])
        dense_all = sb("dense_all", [P, TILES, DENSE])
        low_b = sb("low_b", [P, S * B // P], bf16)
        ids_s = sb("ids_s", [P, TILES, S], i32)
        mask = sb("mask", [P, TILES * S, HIGHS])
        mask_now = [sb(f"mask_now{s}", [P, S, HIGHS]) for s in range(2)]
        low_all = sb("low_all", [P, S * HB], bf16)
        onehot = [sb(f"onehot{s}", [P, 2, S * HB], bf16) for s in range(2)]
        parts = sb("parts", [P, 3, 2 * CAND], bf16)
        prod_flat = prod[:, :, :].rearrange("p k c -> p (k c)")
        tbl_sb = prod_flat[:, 0:2 * CAND]
        ids_f = prod_flat[:, 2 * CAND:2 * CAND + S * B // P].bitcast(i32)
        w1_whole = sb("w1_whole", [P, KT1 * H1])[:, :]
        w2_whole = h2[:, :, :].rearrange("p k c -> p (k c)")[:, 0:KT2 * H2]
        low_dram = nc.dram_tensor("low_dram", (S * B,), bf16).ap()

        cand = pb("cand", [P, 3 * 512])
        pairsT = [pb(f"pairsT{s}", [P, KT1, P]) for s in range(2)]
        dense_ps = [pb(f"dense_ps{s}", [P, GB]) for s in range(2)]
        y_ps = pb("y_ps", [P, GB])

        prep_in = sem("prep_in")
        tbl_in = [sem(f"tbl_in{k}") for k in range(2)]
        weights_in = sem("weights_in")
        small_in = sem("small_in")
        dense_in = sem("dense_in")
        idx_in = [sem(f"idx_in{s}") for s in range(GT)]
        gathered = [sem(f"gathered{s}") for s in range(GT)]
        low_int = sem("low_int")
        low_ready = sem("low_ready")
        low_stored = sem("low_stored")
        low_in = sem("low_in")
        low_1_in = sem("low_1_in")
        high_ready = sem("high_ready")
        mask_ready = sem("mask_ready")
        part_ready = [sem(f"part_ready{k}") for k in range(2)]
        rest_ready = [sem(f"rest_ready{k}") for k in range(2)]
        first_fields_ready = sem("first_fields_ready")
        onehot_ready = [sem(f"onehot_ready{s}") for s in ("_vector", "_scalar")]
        distance_ready = sem("distance_ready")
        cand_ready = sem("cand_ready")
        first_high = sem("first_high")
        carrier = sem("carrier")
        high_kept = sem("high_kept")
        kept = sem("kept")
        wrapped = sem("wrapped")
        tiles_started = sem("tiles_started")
        to_halve = sem("to_halve")
        pool_halved = sem("pool_halved")
        multiplied = sem("multiplied")
        prod_used = sem("prod_used")
        weight_part = sem("weight_part")
        dense_placed = sem("dense_placed")
        feat_first = sem("feat_first")
        feat_out = sem("feat_out")
        h1_first = sem("h1_first")
        h1_out = sem("h1_out")
        dense_done = sem("dense_done")
        dense_out = sem("dense_out")
        y_done = sem("y_done")
        y_out = sem("y_out")
        stored = sem("stored")

        ND = KT2 + KT3

        HALVED = [(q, KT1 - 1) for q in range(1, GT)]
        POOL_HALVED = [(GT - 1, k) for k in range(KT1 - 1)]
        DVE_SHARE = HB
        START_SHARE = 5 * HB
        FIRST_FIELDS = S // 2
        WARM_UP = 16
        WARM_BETWEEN = 12

        def halve_terms(pair):
            return pair[:, :, 0:D // 2], pair[:, :, 0:D // 2], pair[:, :, D // 2:D], ALU.add

        block = ctx.enter_context(nc.Block())

        KINDS = [(0, N_FEW, 0, FEW), (N_FEW, S - N_FEW, COLS_FEW, HIGHS)]

        def candidates(h, f0, n, c0, m):
            return cand[:, c0:c0 + n * m * D].rearrange("p (f h d) -> p f h d", h=m, d=D)[:, :, h, :]

        def rows_of(e, f0, n):
            return e[:, f0 * D:(f0 + n) * D].rearrange("p (f d) -> p f d", d=D)

        @block.sync
        def _(sp):
            idx_t = ids_large.rearrange("(p t) f -> t p f", p=P)
            sp.dma_start(ids_f, ids_flat).then_inc(prep_in, 16)
            for t in range(1, GT):
                sp.dma_start(idx[t][:, :], idx_t[t, :, :]).then_inc(idx_in[t], 16)
            sp.wait_ge(low_ready, 1)
            sp.dma_start(low_dram.rearrange("(p c) -> p c", p=P), low_b[:, :]).then_inc(low_stored, 16)
            sp.wait_ge(low_stored, 16)

            def load_low(h):
                row = low_dram[h * S * HB:(h + 1) * S * HB]
                sp.dma_start(low_all[:, :], row.partition_broadcast(P)).then_inc(low_in, 16)

            load_low(0)
            sp.dma_start(consts_sb[:, :], consts).then_inc(prep_in, 16)
            sp.dma_start(ids_s[:, :, :], ids_small.rearrange("(p t) f -> p t f", p=P)).then_inc(prep_in, 16)
            sp.dma_start(onehot[1][:, 1, :], low_dram[S * HB:2 * S * HB].partition_broadcast(P)).then_inc(low_1_in, 16)
            sp.dma_start(w1_whole.rearrange("p (k n) -> p k n", k=KT1),
                         w1.rearrange("(k p) n -> p k n", p=P)).then_inc(weights_in, 16)
            sp.dma_start(w2_whole.rearrange("p (k n) -> p k n", k=KT2),
                         w2.rearrange("(k p) n -> p k n", p=P)).then_inc(weights_in, 16)
            sp.dma_start(dense_all[:, :, :], dense.rearrange("(p t) f -> p t f", p=P)).then_inc(dense_in, 16)
            sp.dma_start(w3_sb[:, :], w3).then_inc(small_in, 16)
            sp.dma_start(b1_sb[:, :], b1).then_inc(small_in, 16)
            sp.dma_start(b2_sb[:, :], b2).then_inc(small_in, 16)
            for h in range(2, HALVES):
                sp.wait_ge(onehot_ready[0], 2 if h == 2 else 2 * h)
                if h > 2:
                    sp.wait_ge(distance_ready, h - 2)
                load_low(h)
                for t in (2 * h, 2 * h + 1):
                    sp.wait_ge(gathered[t % GT], t // GT * 16 * L)
                    sp.dma_start(idx[t % GT][:, :], idx_t[t, :, :]).then_inc(idx_in[t % GT], 16)
            sp.wait_ge(y_out, GROUPS)
            sp.dma_start(out.rearrange("(p t) o -> p (t o)", p=P), y[:, :]).then_inc(stored, 16)
            sp.wait_ge(stored, 16)

        @block.gpsimd
        def _(pool):
            def gather(g, q):
                pool.wait_ge(multiplied, g * (GT * KT1) + KT1 * (q + 1))
                pool.wait_ge(idx_in[q], g * 16 + 16)
                pool.sem_inc(tiles_started, 1)
                for f in range(L):
                    nc.gpsimd.indirect_dma_start(
                        out=emb[q][:, (S + f) * D:(S + f + 1) * D], out_offset=None, in_=large[f],
                        in_offset=bass.IndirectOffsetOnAxis(ap=idx[q][:, f:f + 1], axis=0),
                    ).then_inc(gathered[q], 16)

            for q in range(GT):
                gather(0, q)
            pool.wait_ge(weight_part, 2)
            nc.gpsimd.tensor_tensor(w1_sb[:, 1, :], w1_whole, w1_sb[:, 0, :].bitcast(fp32),
                                    ALU.subtract).then_inc(weight_part, 1)
            with pool.Fori(1, GROUPS) as g:
                for q in range(GT):
                    gather(g, q)
            for q, k in POOL_HALVED:
                pool.wait_ge(multiplied, ((GROUPS - 1) * GT + q) * KT1 + (GT * KT1 + k + 1))
                pair = prod[:, k, :].rearrange("p (i d) -> p i d", d=D)
                nc.gpsimd.tensor_tensor(*halve_terms(pair)).then_inc(pool_halved, 1)

        def window(t, first, step, count, size):
            a = t[:, :]
            return bass.AP(a.tensor, a.offset + first, [list(a.ap[0]), [step, count], [1, size]])

        @block.vector
        def _(dve):
            dve.sem_inc(multiplied, GT * KT1)
            dve.wait_ge(prep_in, 16)
            nc.vector.tensor_single_scalar(ids_f, ids_f, SPAN - 1, ALU.bitwise_and).then_inc(low_int, 1)
            dve.wait_ge(low_int, 1)
            nc.vector.tensor_copy(low_b[:, :], ids_f).then_inc(low_ready, 1)

            def make_onehot(half, s, cols):
                dve.wait_ge(low_in, half * 16)
                nc.vector.tensor_single_scalar(onehot[s][:, 0, :], low_all[:, :], low_no[:, 0:1],
                                               ALU.is_equal).then_inc(onehot_ready[0], 1)
                nc.vector.tensor_single_scalar(onehot[s][:, 1, 0:cols], low_all[:, 0:cols], low_no[:, 1:2],
                                               ALU.is_equal).then_inc(onehot_ready[0], 1)

            def keep(t, q):
                for h in range(1, HIGHS):
                    if h == 1:
                        dve.wait_ge(first_high, t + 1)
                    else:
                        dve.wait_ge(high_kept, t * (HIGHS - 2) + (h - 1))
                    dve.sem_inc(carrier, 1)
                    for f0, n, c0, m in KINDS:
                        if h < m:
                            last = nc.vector.copy_predicated(
                                rows_of(emb[q], f0, n),
                                mask_now[q % 2][:, f0:f0 + n, h].unsqueeze(2).to_broadcast([P, n, D]).bitcast(i32),
                                candidates(h, f0, n, c0, m))
                    last.then_inc(kept if h == HIGHS - 1 else high_kept, 1)

            def multiply(t, q, k, halved_no=None):
                e = emb[q]
                dve.wait_ge(prod_used, t * KT1 + (k + 1))
                first = (k * SHIFTS + 1) * D
                whole = SHIFTS if k < KT1 - 1 else SHIFTS - 1
                last = nc.vector.tensor_tensor(
                    prod[:, k, 0:whole * ROW].rearrange("p (k r) -> p k r", r=ROW),
                    window(e, 0, 0, whole, ROW), window(e, first, D, whole, ROW), ALU.mult)
                if whole < SHIFTS:
                    last = nc.vector.tensor_tensor(prod[:, k, whole * ROW:whole * ROW + ROW // 2],
                                                   e[:, 0:ROW // 2], e[:, ROW // 2:ROW], ALU.mult)
                if halved_no is None:
                    last.then_inc(multiplied, 1)
                    return
                last.then_inc(to_halve, 1)
                dve.wait_ge(to_halve, halved_no)
                pair = prod[:, k, 0:whole * ROW + (0 if whole == SHIFTS else ROW // 2)].rearrange("p (i d) -> p i d", d=D)
                nc.vector.tensor_tensor(*halve_terms(pair)).then_inc(multiplied, 1)

            def second_feat(t, g, q):
                dve.wait_ge(feat_first, t + 1)
                at = slice(q * P, (q + 1) * P)
                nc.vector.tensor_tensor(feat[:, 1, :, :, at][:, g % 2, :, :], pairsT[q % 2][:, :, :],
                                        feat[:, 0, :, :, at][:, g % 2, :, :].bitcast(fp32),
                                        ALU.subtract).then_inc(feat_out, 1)

            def second_h1(G, n):
                dve.wait_ge(h1_first, G * KT2 + (n + 1))
                nc.vector.tensor_tensor(h1[:, 1, n, :], h1_whole[n % 2][:, :], h1[:, 0, n, :].bitcast(fp32),
                                        ALU.subtract).then_inc(h1_out, 1)

            for k in range(2):
                half = slice(k * CAND, (k + 1) * CAND)
                dve.wait_ge(part_ready[k], 1)
                nc.vector.tensor_tensor(tbl_sb[:, half], tbl_sb[:, half], parts[:, 0, half],
                                        ALU.subtract).then_inc(rest_ready[k], 1)
            for k in range(2):
                half = slice(k * CAND, (k + 1) * CAND)
                dve.wait_ge(rest_ready[k], 1)
                dve.wait_ge(part_ready[k], 2)
                nc.vector.tensor_tensor(parts[:, 2, half], tbl_sb[:, half], parts[:, 1, half],
                                        ALU.subtract).then_inc(part_ready[k], 1)
            dve.wait_ge(prep_in, 3 * 16)
            dve.wait_ge(low_in, 16)
            for cols, signal in ((slice(0, FIRST_FIELDS * HB), first_fields_ready),
                                 (slice(FIRST_FIELDS * HB, S * HB), onehot_ready[0])):
                for k in range(2):
                    nc.vector.tensor_single_scalar(onehot[0][:, k, cols], low_all[:, cols], low_no[:, k:k + 1],
                                                   ALU.is_equal).then_inc(signal, 1)
            nc.vector.tensor_single_scalar(ids_s[:, :, :], ids_s[:, :, :], SPAN.bit_length() - 1,
                                           ALU.logical_shift_right).then_inc(high_ready, 1)
            dve.wait_ge(high_ready, 1)
            nc.vector.tensor_tensor(
                mask[:, :, :], ids_s[:, :, :].rearrange("p t f -> p (t f)").unsqueeze(2).to_broadcast([P, TILES * S, HIGHS]),
                high_no.unsqueeze(1).to_broadcast([P, TILES * S, HIGHS]), ALU.is_equal).then_inc(mask_ready, 1)
            keep(0, 0)
            dve.wait_ge(low_1_in, 16)
            for k in range(2):
                nc.vector.tensor_single_scalar(onehot[1][:, k, :], onehot[1][:, 1, :], low_no[:, k:k + 1],
                                               ALU.is_equal).then_inc(onehot_ready[0], 1)

            def group(g, first, last):
                def products(t, q, k):
                    halve = not first and (q, k) in HALVED
                    multiply(t, q, k, (g - 1) * len(HALVED) + (HALVED.index((q, k)) + 1) if halve else None)

                for q in range(GT):
                    t = g * GT + q
                    dve.wait_ge(wrapped, t + 1)
                    dve.wait_ge(gathered[q], g * (16 * L) + 16 * L)
                    products(t, q, 0)
                    if first and q == 0:
                        keep(1, 1)
                    products(t, q, 1)
                    if first and q == 1:
                        keep(3, 3)
                    if q % 2 == 0 and not last:
                        dve.wait_ge(cand_ready, t + 2)
                        make_onehot(g * 2 + (q // 2 + 2), q // 2, START_SHARE if first and q == 0 else DVE_SHARE)
                    if not first and q == 2:
                        second_h1(g - 1, 0)
                        second_h1(g - 1, 1)
                    products(t, q, 2)
                    products(t, q, 3)
                    if first and q == 0:
                        nc.vector.memset(prod[:, KT1 - 1, (P - DENSE) * D:P * D], 0.0).then_inc(dense_placed, 1)
                    if q:
                        second_feat(t - 1, g, q - 1)
                    elif not first:
                        second_feat(t - 1, g - 1, GT - 1)
                    if not first and q == 2:
                        second_h1(g - 1, 2)
                        second_h1(g - 1, 3)
                    if first and q == 0:
                        keep(2, 2)
                    elif not (last and q):
                        keep(t + AHEAD, (q + AHEAD) % GT)
                    if first and q == GT - 1:
                        dve.wait_ge(weight_part, 2)
                        nc.vector.tensor_tensor(w2_sb[:, 1, :], w2_whole, w2_sb[:, 0, :].bitcast(fp32),
                                                ALU.subtract).then_inc(weight_part, 1)

            group(0, True, False)
            with dve.Fori(1, GROUPS - 1) as g:
                group(g, False, False)
            group(GROUPS - 1, False, True)
            second_feat(TILES - 1, GROUPS - 1, GT - 1)
            for n in range(KT2):
                second_h1(GROUPS - 1, n)

        @block.tensor
        def _(pe):
            pe.sem_inc(prod_used, KT1)

            def look_up(t, q, half):
                whole = not isinstance(t, int) or t > 0
                if whole:
                    pe.wait_ge(onehot_ready[0], t + 2 - q % 2)
                else:
                    pe.wait_ge(first_fields_ready, 2)
                if not isinstance(half, int) or half >= 2:
                    pe.wait_ge(onehot_ready[1], half - 1)
                pe.wait_ge(kept, t + 1)
                s, c = q // 2, (q % 2) * P
                for f in range(S):
                    if not whole and f == FIRST_FIELDS:
                        pe.wait_ge(onehot_ready[0], 2)
                    for k in range(2):
                        for part in range(3):
                            last = nc.tensor.matmul(
                                cand[:, OFF[f]:OFF[f] + widths[f]],
                                onehot[s][:, k, f * HB + c:f * HB + c + P],
                                parts[:, part, k * CAND + OFF[f]:k * CAND + OFF[f] + widths[f]],
                                start=(k == 0 and part == 0), stop=(k == 1 and part == 2))
                last.then_inc(cand_ready, 1)

            def transpose_and_sum(t, q, first_group, last_group):
                pe.wait_ge(feat_out, t + 1)
                for k in range(KT1):
                    if k == KT1 - 1:
                        pe.wait_ge(dense_placed, t + 2)
                    pe.wait_ge(multiplied, t * KT1 + (GT * KT1 + k + 1))
                    src = prod[:, k, :].rearrange("p (q d) -> p d q", d=D)
                    terms = D // 2 if not first_group and (q, k) in HALVED else D
                    if last_group and (q, k) in POOL_HALVED:
                        terms = D // 2
                        pe.wait_ge(pool_halved, POOL_HALVED.index((q, k)) + 1)
                    for d in range(terms):
                        last = nc.tensor.matmul(pairsT[q % 2][:, k, :], src[:, d, :], ident, is_transpose=True,
                                                start=(d == 0), stop=(d == terms - 1))
                    last.then_inc(prod_used, 1)

            def product(ps, w, x, n, m, kt, before=lambda k: None):
                for k in range(kt):
                    before(k)
                    for i, j in ((0, 0), (0, 1), (1, 0)):
                        last = nc.tensor.matmul(ps[:, :], w[:, i, k * n + m * P:k * n + (m + 1) * P], x(j, k),
                                                start=(k + i + j == 0), stop=(k == kt - 1 and i == 1))
                last.then_inc(dense_done, 1)

            def layer_12(G, n):
                pe.wait_ge(dense_out, G * ND + (n + 1))
                if n < KT2:
                    if n == 0:
                        pe.wait_ge(feat_out, G * GT + (GT + 2))
                    product(dense_ps[n % 2], w1_sb, lambda j, k: feat[:, j, :, k, :][:, G % 2, :], H1, n, KT1)
                else:
                    product(dense_ps[n % 2], w2_sb, lambda j, k: h1[:, j, k, :], H2, n - KT2, KT2,
                            lambda k: pe.wait_ge(h1_out, G * KT2 + (k + 3)))

            def layer_3(G):
                pe.wait_ge(dense_out, G * ND + (ND + 2))
                for q in range(GT):
                    for k in range(KT3):
                        last = nc.tensor.matmul(y_ps[:, q:q + 1], h2[:, k, q * P:(q + 1) * P], w3_sb[:, k:k + 1],
                                                start=(k == 0), stop=(k == KT3 - 1))
                last.then_inc(y_done, 1)

            def dense_piece(G, q):
                if q < GT - 1:
                    layer_12(G, 2 * q)
                    layer_12(G, 2 * q + 1)
                else:
                    layer_3(G)

            def stay_warm(count):
                for _ in range(count):
                    nc.tensor.matmul(y_ps[:, :], parts[:, 0, 0:P], parts[:, 0, 0:GB], start=True, stop=True)

            pe.wait_ge(part_ready[0], 2)
            stay_warm(WARM_UP)
            for k in range(2):
                pe.wait_ge(part_ready[k], 3)
            for t in range(AHEAD):
                look_up(t, t, t // 2)
                if t < AHEAD - 1:
                    stay_warm(WARM_BETWEEN)
            pe.wait_ge(small_in, 3 * 16)
            pe.wait_ge(prep_in, 3 * 16)

            def group(g, first, last):
                for q in range(GT):
                    t = g * GT + q
                    if first and q == 0:
                        transpose_and_sum(t, q, first, last)
                        look_up(AHEAD, AHEAD, AHEAD // 2)
                        stay_warm(WARM_BETWEEN)
                        continue
                    if not (last and q):
                        look_up(t + AHEAD, (q + AHEAD) % GT, g * 2 + (q + AHEAD) // 2)
                    transpose_and_sum(t, q, first, last)
                    if not first:
                        dense_piece(g - 1, q)

            group(0, True, False)
            pe.wait_ge(weight_part, 4)
            with pe.Fori(1, GROUPS - 1) as g:
                group(g, False, False)
            group(GROUPS - 1, False, True)
            for q in range(GT):
                dense_piece(GROUPS - 1, q)

        @block.scalar
        def _(act):
            act.sem_inc(feat_out, 2)
            act.sem_inc(kept, 1)
            act.sem_inc(dense_out, 2)
            act.sem_inc(h1_out, 2)
            act.dma_start(idx[0][:, :], ids_large.rearrange("(p t) f -> t p f", p=P)[0, :, :]).then_inc(idx_in[0], 16)
            for k in range(2):
                half = slice(k * CAND, (k + 1) * CAND)
                act.dma_start(tbl_sb[:, half], tbl[:, half]).then_inc(tbl_in[k], 16)
            for k in range(2):
                half = slice(k * CAND, (k + 1) * CAND)
                act.wait_ge(tbl_in[k], 16)
                nc.scalar.copy(parts[:, 0, half], tbl_sb[:, half]).then_inc(part_ready[k], 1)
            for k in range(2):
                half = slice(k * CAND, (k + 1) * CAND)
                act.wait_ge(rest_ready[k], 1)
                nc.scalar.copy(parts[:, 1, half], tbl_sb[:, half]).then_inc(part_ready[k], 1)

            def start_keeping(t, q):
                act.wait_ge(kept, t + 1)
                nc.scalar.copy(mask_now[q % 2][:, :, :],
                               mask[:, :, :].rearrange("p (t f) h -> p t f h", f=S)[:, t, :, :])
                act.wait_ge(cand_ready, t + 1)
                act.wait_ge(multiplied, t * KT1 + KT1)
                for f0, n, c0, m in KINDS:
                    last = nc.scalar.copy(rows_of(emb[q], f0, n), candidates(0, f0, n, c0, m))
                last.then_inc(first_high, 1)

            def near_one(half, s, from_col):
                part = onehot[s][:, 1, from_col:S * HB]
                act.wait_ge(low_in, half * 16)
                nc.scalar.activation(part, low_all[:, from_col:S * HB], ACT.Abs, bias=minus_low_no
                                     ).then_inc(distance_ready, 1)
                act.wait_ge(distance_ready, half - 1)
                nc.scalar.activation(part, part, ACT.Relu, bias=one, scale=-1.0).then_inc(onehot_ready[1], 1)

            def wrap(t, q):
                act.wait_ge(kept, t + 2)
                nc.scalar.copy(emb[q][:, ROW:ROW + WRAP * D], emb[q][:, 0:WRAP * D]).then_inc(wrapped, 1)

            def place_dense(t):
                act.wait_ge(prod_used, t * KT1 + KT1)
                nc.scalar.copy(prod[:, KT1 - 1, (P - DENSE) * D:P * D].rearrange("p (f d) -> p f d", d=D)[:, :, 0],
                               dense_all[:, t, :]).then_inc(dense_placed, 1)

            def first_feat(t, g, q):
                act.wait_ge(prod_used, t * KT1 + 2 * KT1)
                nc.scalar.copy(feat[:, 0, :, :, q * P:(q + 1) * P][:, g % 2, :, :], pairsT[q % 2][:, :, :]
                               ).then_inc(feat_first, 1)

            def dense_piece(G, q):
                if q < GT - 1:
                    for n in (2 * q, 2 * q + 1):
                        act.wait_ge(dense_done, G * ND + (n + 1))
                        if n < KT2:
                            act.wait_ge(h1_out, G * KT2 + (n + 1))
                            nc.scalar.activation(h1_whole[n % 2][:, :], dense_ps[n % 2][:, :], ACT.Relu,
                                                 bias=b1_sb[:, n:n + 1]).then_inc(dense_out, 1)
                            act.wait_ge(dense_out, G * ND + (n + 3))
                            nc.scalar.copy(h1[:, 0, n, :], h1_whole[n % 2][:, :]).then_inc(h1_first, 1)
                        else:
                            m = n - KT2
                            nc.scalar.activation(h2[:, m, :], dense_ps[n % 2][:, :], ACT.Relu,
                                                 bias=b2_sb[:, m:m + 1]).then_inc(dense_out, 1)
                else:
                    act.wait_ge(y_done, G + 1)
                    nc.scalar.copy(y[:, bass.ts(G, GT)], y_ps[:, 0:GT]).then_inc(y_out, 1)

            act.wait_ge(mask_ready, 1)
            start_keeping(0, 0)
            wrap(0, 0)
            start_keeping(1, 1)
            near_one(2, 0, START_SHARE)
            act.wait_ge(dense_in, 16)

            def group(g, first, last):
                for q in range(GT):
                    t = g * GT + q
                    if first and q == 0:
                        wrap(1, 1)
                        start_keeping(2, 2)
                        act.wait_ge(dense_placed, 1)
                    place_dense(t)
                    if first and q < 2:
                        wrap(q + 2, q + 2)
                    if first and q == 1:
                        act.wait_ge(weights_in, 2 * 16)
                        for w, whole in ((w1_sb, w1_whole), (w2_sb, w2_whole)):
                            nc.scalar.copy(w[:, 0, :], whole).then_inc(weight_part, 1)
                    if not (last and q):
                        start_keeping(t + AHEAD, (q + AHEAD) % GT)
                    if q % 2 == 0 and not last and not (first and q == 0):
                        near_one(g * 2 + (q // 2 + 2), q // 2, DVE_SHARE)
                    if not (last and q or first and q == 0):
                        wrap(t + AHEAD, (q + AHEAD) % GT)
                    first_feat(t, g, q)
                    if not first:
                        dense_piece(g - 1, q)

            act.wait_ge(small_in, 3 * 16)
            group(0, True, False)
            with act.Fori(1, GROUPS - 1) as g:
                group(g, False, False)
            group(GROUPS - 1, False, True)
            for q in range(GT):
                dense_piece(GROUPS - 1, q)


def kernel(**inputs):
    import numpy as np
    import concourse.bacc as bacc
    from concourse import mybir
    from concourse.bass_utils import run_bass_kernel_spmd as run

    ids = np.asarray(inputs["ids"])
    B, F = ids.shape
    tables = [np.asarray(inputs[f"tbl_{f}"]) for f in range(F)]
    D = tables[0].shape[1]
    small, large = field_order([t.shape[0] for t in tables])
    order = small + large
    row_of = {}
    for i in range(F - 1):
        for j in range(i + 1, F):
            row_of[i, j] = len(row_of)
    w1 = np.asarray(inputs["W_top1"])
    rows = [row_of[min(order[i], order[j]), max(order[i], order[j])] for i, j in shifted_pairs(F)]
    rows += range(len(rows), w1.shape[0])

    highs = [-(-tables[f].shape[0] // SPAN) for f in small]
    blocks = []
    for f, n in zip(small, highs):
        padded = np.zeros((n * SPAN, D), np.float32)
        padded[:tables[f].shape[0]] = tables[f]
        blocks.append(padded.reshape(n, 2, P, D).transpose(2, 1, 0, 3).reshape(P, 2, n * D))
    tbl = np.concatenate(blocks, axis=2)

    HB = 2 * P
    ids_flat = np.ascontiguousarray(ids[:, small].reshape(P, B // HB, 2, len(small)).transpose(1, 3, 2, 0)).reshape(P, -1)
    consts = np.zeros((P, P + 4 + max(highs)), np.float32)
    consts[:, :P] = np.eye(P, dtype=np.float32)
    consts[:, P] = np.arange(P)
    consts[:, P + 1] = np.arange(P, 2 * P)
    consts[:, P + 2] = -consts[:, P + 1]
    consts[:, P + 3] = 1
    consts[:, P + 4:] = np.arange(max(highs))
    b1, b2, w3 = (np.asarray(inputs[k]) for k in ("b_top1", "b_top2", "W_top3"))
    host = {
        "dense": np.asarray(inputs["dense_ctx"]),
        "ids_flat": ids_flat,
        "ids_small": np.ascontiguousarray(ids[:, small]),
        "ids_large": np.ascontiguousarray(ids[:, large]),
        "tbl": tbl.reshape(P, -1),
        "w1": np.ascontiguousarray(w1[rows]),
        "b1": np.ascontiguousarray(b1.reshape(-1, P).T),
        "w2": np.asarray(inputs["W_top2"]),
        "b2": np.ascontiguousarray(b2.reshape(-1, P).T),
        "w3": np.ascontiguousarray(w3.reshape(-1, P).T),
        "consts": consts,
    }
    names = list(host)
    for f in large:
        host[f"tbl_{f}"] = tables[f]

    nc = bacc.Bacc("TRN2", target_bir_lowering=False, num_devices=1)
    ap = {k: nc.dram_tensor(f"in_{k}", v.shape, mybir.dt.from_np(v.dtype), kind="ExternalInput").ap()
          for k, v in host.items()}
    out = nc.dram_tensor("out_y", (B, 1), mybir.dt.float32, kind="ExternalOutput").ap()
    build(nc, ap["dense"], ap["ids_flat"], ap["ids_small"], ap["ids_large"], [ap[f"tbl_{f}"] for f in large],
          ap["tbl"], [n * D for n in highs], ap["w1"], ap["b1"], ap["w2"], ap["b2"], ap["w3"], ap["consts"], out)
    r = run(nc, [{f"in_{k}": v for k, v in host.items()}], core_ids=[0])
    return r.results[0]["out_y"]
```
